# Optimizing a Trainium2 kernel written in Bass

```python
import numpy as np
import jax
import jax.numpy as jnp

def _softmax(x, axis=-1):
    return jax.nn.softmax(x, axis=axis)

def _gelu(x):
    return jax.nn.gelu(x, approximate=True)

def _silu(x):
    return jax.nn.silu(x)

def _sigmoid(x):
    return jax.nn.sigmoid(x)

def _layernorm(x, axis=-1, eps=1e-05):
    m = jnp.mean(x, axis=axis, keepdims=True)
    v = jnp.var(x, axis=axis, keepdims=True)
    return (x - m) / jnp.sqrt(v + eps)

def _scatter_add(tgt, idx, src, axis=0):
    return tgt.at[idx].add(src)

def _segment_sum(src, seg, n):
    return jax.ops.segment_sum(src, seg, n)
kernel_name = 'mk_cond_resid_d2_seqx_r2_655991'

def setup_inputs(seed: int=0):
    np.random.seed(seed)
    _w = jnp.asarray

    def _rec_inputs():
        import jax
        import jax.numpy as jnp
        _rk = jax.random.key(seed)
        x = -0.0003929 + 0.9999 * jax.random.normal(jax.random.fold_in(_rk, 1), (64, 128, 512), jnp.float32)
        _lenS = 128 - jax.random.randint(jax.random.fold_in(_rk, 7), (64,), 0, max(1, 128 // 4) + 1, jnp.int32)
        _lenS2 = 128 - jax.random.randint(jax.random.fold_in(_rk, 8), (64,), 0, max(1, 128 // 4) + 1, jnp.int32)
        itok_B_0_2 = jax.random.randint(jax.random.fold_in(_rk, 11), (64,), 0, 3, jnp.int32)
        itok_B_0_63 = jax.random.randint(jax.random.fold_in(_rk, 12), (64,), 0, 64, jnp.int32)
        return (x, itok_B_0_2, itok_B_0_63)
    x, itok_B_0_2, itok_B_0_63 = _rec_inputs()

    def _L0_cond_setup():
        import jax, jax.numpy as jnp
        import numpy as np
        NEG_INF = -1e+30
        key = jax.random.key(seed)
        k1, k2, k3, k4, k5 = jax.random.split(key, 5)
        B, S, D, A = (16, 512, 512, 128)
        hidden = jax.random.normal(k1, (B, S, D), dtype=jnp.float32)
        W1 = jax.random.normal(k2, (D, A), dtype=jnp.float32) / np.sqrt(D)
        b1 = jax.random.normal(k3, (A,), dtype=jnp.float32) * 0.01
        v = jax.random.normal(k4, (A,), dtype=jnp.float32) / np.sqrt(A)
        prompt_type_ids = jax.random.randint(k5, (B,), 0, 3, dtype=jnp.int32)
        return {'hidden': hidden, 'W1': W1, 'b1': b1, 'v': v, 'prompt_type_ids': prompt_type_ids}
    _L0_cond_all = _L0_cond_setup()
    _L0_cond_in = {k: v for k, v in _L0_cond_all.items() if k in ('W1', 'b1', 'v')}
    del _L0_cond_all

    def _L1_cond_setup():
        import jax, jax.numpy as jnp
        import numpy as np
        NUM_CATEGORIES = 64
        INPUT_DIM = 512
        HIDDEN_DIM = 512
        B = 128
        S = 64
        key = jax.random.key(seed)
        kx, kc, kw = jax.random.split(key, 3)
        x = jax.random.normal(kx, (B, S, INPUT_DIM), dtype=jnp.float32)
        cat_ids = jax.random.randint(kc, (B,), 0, NUM_CATEGORIES, dtype=jnp.int32)
        W = 0.02 * jax.random.normal(kw, (NUM_CATEGORIES, INPUT_DIM, HIDDEN_DIM), dtype=jnp.float32)
        b = jnp.zeros((NUM_CATEGORIES, HIDDEN_DIM), dtype=jnp.float32)
        return {'x': x, 'cat_ids': cat_ids, 'W': W, 'b': b}
    _L1_cond_all = _L1_cond_setup()
    _L1_cond_in = {k: v for k, v in _L1_cond_all.items() if k in ('W', 'b')}
    del _L1_cond_all
    return {'x': x, 'itok_B_0_2': itok_B_0_2, 'itok_B_0_63': itok_B_0_63, 'L0_cond_W1': _L0_cond_in['W1'], 'L0_cond_b1': _L0_cond_in['b1'], 'L0_cond_v': _L0_cond_in['v'], 'L1_cond_W': _L1_cond_in['W'], 'L1_cond_b': _L1_cond_in['b']}

def reference(x, itok_B_0_2, itok_B_0_63, L0_cond_W1, L0_cond_b1, L0_cond_v, L1_cond_W, L1_cond_b):
    import jax
    import jax.numpy as jnp

    def _L0_cond_ref(hidden, W1, b1, v, prompt_type_ids):
        import jax, jax.numpy as jnp
        import numpy as np
        NEG_INF = -1e+30
        B, S, D = hidden.shape
        attn_in = jnp.tanh(jnp.einsum('bsd,da->bsa', hidden, W1) + b1)
        scores = jnp.einsum('bsa,a->bs', attn_in, v)
        idx = jnp.arange(S)
        j = idx[:, None]
        l = idx[None, :]
        prefix_m = l <= j
        postfix_m = l >= j
        cloze_m = l != j
        pt = prompt_type_ids[:, None, None]
        mask = jnp.where(pt == 0, prefix_m[None], jnp.where(pt == 1, postfix_m[None], cloze_m[None]))
        masked_scores = jnp.where(mask, scores[:, None, :], NEG_INF)
        p = jax.nn.softmax(masked_scores, axis=-1)
        cnt = jnp.sum(mask, axis=-1).astype(hidden.dtype)
        pooled = jnp.einsum('bjl,bld->bjd', p, hidden) / cnt[..., None]
        return pooled

    def _L1_cond_ref(x, cat_ids, W, b):
        import jax, jax.numpy as jnp
        import numpy as np
        NUM_CATEGORIES = 64
        INPUT_DIM = 512
        HIDDEN_DIM = 512
        B = 128
        S = 64
        selected_W = W[cat_ids]
        selected_b = b[cat_ids]
        out = jnp.einsum('bsd,bdh->bsh', x, selected_W) + selected_b[:, None, :]
        return out
    x = x + _L0_cond_ref(x, L0_cond_W1, L0_cond_b1, L0_cond_v, itok_B_0_2)
    x = x + _L1_cond_ref(x, itok_B_0_63, L1_cond_W, L1_cond_b)
    return x

_drawn_inputs = setup_inputs


def setup_inputs(seed=0):
    import zlib

    import numpy as np

    out = dict(_drawn_inputs(seed))
    spreads = {'L1_cond_b': (0.0, 0.1)}
    factors = {'L0_cond_W1': 4.115, 'L0_cond_b1': 8.0, 'L0_cond_v': 3.449}
    for name, (base, spread) in spreads.items():
        noise = np.random.default_rng([zlib.crc32(name.encode()), seed]).standard_normal(out[name].shape)
        drawn = base * np.exp(spread * noise) if base else spread * noise
        out[name] = jnp.asarray(drawn.astype(out[name].dtype))
    for name, factor in factors.items():
        out[name] = (out[name] * factor).astype(out[name].dtype)
    return out
```

```python
from contextlib import ExitStack

import concourse.bass as bass
from concourse import mybir

ALU = mybir.AluOpType
ACT = mybir.ActivationFunctionType
AXIS_X = mybir.AxisListType.X
F32 = mybir.dt.float32
F32R = mybir.dt.float32r
BF16 = mybir.dt.bfloat16
I32 = mybir.dt.int32

MASKED = -1e30


def program(nc, x, types, cats, w1, b1, v, w, bias, out):
    B, S, D = x.shape
    A = w1.shape[1]
    C = w.shape[0]
    P = 128
    assert S == P and A == P and D % P == 0
    DC = D // P
    HALF = DC // 2
    G = 4
    TURN = 2 * G
    GROUPS = B // G
    TURNS = B // TURN
    NX, NW, NZ, NO, NB = TURN, 4, 2, 4, 4

    ctx = ExitStack()
    with ctx:
        def sb(name, shape, dt):
            return ctx.enter_context(nc.sbuf_tensor(name, shape, dt))

        def bank(name):
            return ctx.enter_context(nc.psum_tensor(name, [P, 512], F32))

        def sem(name):
            return ctx.enter_context(nc.semaphore(name))

        x_sb = [sb(f"x_sb{i}", [P, D], F32) for i in range(NX)]
        z_sb = [sb(f"z_sb{i}", [P, D], F32) for i in range(NZ)]
        z_hi = [sb(f"z_hi{i}", [P, D], F32R) for i in range(NZ)]
        z_lo = [sb(f"z_lo{i}", [P, D], F32R) for i in range(NZ)]
        out_sb = [sb(f"out_sb{i}", [P, D], F32) for i in range(NO)]
        xT_hi = [sb(f"xT_hi{i}", [P, DC, G * S], F32R) for i in range(2)]
        xT_lo = [sb(f"xT_lo{i}", [P, DC, G * S], F32R) for i in range(2)]
        w_raw = [sb(f"w_raw{i}", [P, DC, D], F32) for i in range(NW)]
        w_hi = [sb(f"w_hi{i}", [P, DC, D], F32R) for i in range(NW)]
        w_lo = [sb(f"w_lo{i}", [P, DC, D], F32R) for i in range(NW)]
        bias_rows = [sb(f"bias_rows{i}", [2, D], F32R) for i in range(NB)]
        attn = sb("attn", [P, G * S], F32)
        probs = sb("probs", [P, G, S], F32)
        mix = sb("mix", [P, G, S], F32)
        mix_hi = [sb(f"mix_hi{i}", [P, G, S], F32R) for i in range(2)]
        mix_lo = [sb(f"mix_lo{i}", [P, G, S], F32R) for i in range(2)]
        neg_max = sb("neg_max", [P, G], F32)
        row_sum = sb("row_sum", [P, G], F32)
        row_div = sb("row_div", [P, G], F32)
        row_scale = sb("row_scale", [P, G], F32)

        w1_raw = sb("w1_raw", [P, DC, A], F32)
        w1_hi = sb("w1_hi", [P, DC, A], F32R)
        w1_lo = sb("w1_lo", [P, DC, A], F32R)
        b1_col = sb("b1_col", [P, 1], F32)
        v_col = sb("v_col", [P, 1], F32)
        v_wide = sb("v_wide", [P, P], F32)
        ident = sb("ident", [P, P], F32)
        ident_bf = sb("ident_bf", [P, P], BF16)
        penalty = sb("penalty", [P, 3, S], BF16)
        ones = sb("ones", [2, P], F32R)
        b_raw = sb("b_raw", [C, D], F32)
        b_hi = sb("b_hi", [C, D], F32R)
        b_lo = sb("b_lo", [C, D], F32R)
        cat_row = sb("cat_row", [1, B], I32)
        type_all = sb("type_all", [P, B], I32)
        is_prefix = sb("is_prefix", [P, B], F32)
        is_postfix = sb("is_postfix", [P, B], F32)
        type_tmp = sb("type_tmp", [P, B], F32)
        type_row = sb("type_row", [1, B], I32)
        row_i = sb("row_i", [P, 2], I32)
        row_f = sb("row_f", [P, 2], F32)
        seen = sb("seen", [P, B], F32)
        b_split = nc.dram_tensor("b_split", (C, 2, D), F32, kind="Internal").ap()

        ps_xT = [bank("ps_xT0"), bank("ps_xT1")]
        ps_mix = bank("ps_mix")
        ps_scores = bank("ps_scores")
        ps_xw = [bank("ps_xw0"), bank("ps_xw1")]
        ps_pz = [bank("ps_pz0"), bank("ps_pz1")]

        small_in = [sem(f"small_in{i}") for i in range(6)]
        x_in = [sem(f"x_in{i}") for i in range(NX)]
        w_in = [sem(f"w_in{i}") for i in range(NW)]
        bias_in = [sem(f"bias_in{i}") for i in range(NB)]
        out_stored = [sem(f"out_stored{i}") for i in range(NO)]
        b_split_stored = sem("b_split_stored")
        pool_step = sem("pool_step")
        consts_ready = sem("consts_ready")
        setup_step = sem("setup_step")
        b_hi_ready = sem("b_hi_ready")
        b_parts_ready = sem("b_parts_ready")
        w1_hi_ready = sem("w1_hi_ready")
        pe_consts_ready = sem("pe_consts_ready")
        xT_done = sem("xT_done")
        xT_hi_ready = sem("xT_hi_ready")
        xT_lo_ready = sem("xT_lo_ready")
        w_hi_ready = sem("w_hi_ready")
        w_lo_ready = sem("w_lo_ready")
        pre_done = sem("pre_done")
        attn_ready = sem("attn_ready")
        scores_done = sem("scores_done")
        neg_max_ready = sem("neg_max_ready")
        exp_ready = sem("exp_ready")
        div_ready = sem("div_ready")
        scale_ready = sem("scale_ready")
        probs_ready = sem("probs_ready")
        probsT_done = sem("probsT_done")
        mix_ready = sem("mix_ready")
        mix_hi_ready = sem("mix_hi_ready")
        mix_lo_ready = sem("mix_lo_ready")
        xw_done = sem("xw_done")
        z_ready = sem("z_ready")
        z_hi_ready = sem("z_hi_ready")
        z_lo_ready = sem("z_lo_ready")
        pz_done = sem("pz_done")
        out_ready = sem("out_ready")

        block = ctx.enter_context(nc.Block())

        def turns(eng, body):
            body(0, 0, True, False)
            with eng.Fori(1, TURNS - 1) as t:
                body(t, TURN * t, False, False)
            body(TURNS - 1, TURN * (TURNS - 1), False, True)

        @block.sync
        def _(sp):
            def load_x(n, slot):
                sp.dma_start(x_sb[slot][:], x[bass.ds(n, 1)].rearrange("a s d -> (a s) d"))\
                    .then_inc(x_in[slot], 16)

            def load_w(cat, slot):
                sp.dma_start(w_raw[slot][:], w[bass.ds(cat, 1)].rearrange("a (c p) h -> p (a c) h", p=P))\
                    .then_inc(w_in[slot], 16)

            def load_bias(cat, slot):
                sp.dma_start(bias_rows[slot][:].bitcast(F32), b_split[bass.ds(cat, 1)].rearrange("a t h -> (a t) h"))\
                    .then_inc(bias_in[slot], 16)

            sp.dma_start(cat_row[:], cats.rearrange("(a n) -> a n", a=1)).then_inc(small_in[0], 16)
            load_x(0, 0)
            sp.dma_start(type_all[:], types.rearrange("(a n) -> a n", a=1).to_broadcast([P, B]))\
                .then_inc(small_in[4], 16)
            load_x(1, 1)
            sp.dma_start(v_col[:], v.rearrange("(p a) -> p a", a=1)).then_inc(small_in[3], 16)
            sp.dma_start(w1_raw[:], w1.rearrange("(c p) a -> p c a", p=P)).then_inc(small_in[1], 16)
            load_x(2, 2)
            load_x(3, 3)
            sp.wait_ge(small_in[0], 16)
            first_cats = [sp.value_load(cat_row[0:1, 0:1], min_val=0, max_val=C - 1)]
            load_w(first_cats[0], 0)
            first_cats += [sp.value_load(cat_row[0:1, k:k + 1], min_val=0, max_val=C - 1)
                           for k in range(1, NW + 2)]
            sp.dma_start(b_raw[:], bias).then_inc(small_in[5], 16)
            sp.dma_start(b1_col[:], b1.rearrange("(p a) -> p a", a=1)).then_inc(small_in[2], 16)
            load_w(first_cats[1], 1)
            load_x(4, 4)
            load_x(5, 5)
            load_w(first_cats[2], 2)
            sp.wait_ge(b_parts_ready, 1)
            sp.dma_start(b_split[:, 0, :], b_hi[:].bitcast(F32)).then_inc(b_split_stored, 16)
            sp.dma_start(b_split[:, 1, :], b_lo[:].bitcast(F32)).then_inc(b_split_stored, 16)
            load_x(6, 6)
            load_x(7, 7)
            load_w(first_cats[3], 3)
            for k in range(2):
                sp.wait_ge(w_lo_ready, 2 * k + 2)
                load_w(first_cats[NW + k], k)
            sp.wait_ge(b_split_stored, 32)
            load_bias(first_cats[0], 0)

            def body(t, k0, first, last):
                for s in range(TURN):
                    k = k0 + s
                    has_w = not (last and s + NW + 2 >= TURN)
                    has_bias = not (last and s + 1 >= TURN)
                    if has_w:
                        w_cat = sp.value_load(cat_row[0:1, bass.ds(k + NW + 2, 1)], min_val=0, max_val=C - 1)
                    if has_bias:
                        bias_cat = sp.value_load(cat_row[0:1, bass.ds(k + 1, 1)], min_val=0, max_val=C - 1)
                    if not (first and s == 0) and not (last and s + NX - 1 >= TURN):
                        sp.wait_ge(z_ready, k)
                        load_x(k + NX - 1, (s - 1) % NX)
                    if not first or s >= 3:
                        sp.wait_ge(out_ready, k - 2)
                        sp.dma_start(out[bass.ds(k - 3, 1)].rearrange("a s d -> (a s) d"),
                                     out_sb[(s - 3) % NO][:]).then_inc(out_stored[(s - 3) % NO], 16)
                    if has_bias:
                        load_bias(bias_cat, (s + 1) % NB)
                    if has_w:
                        sp.wait_ge(w_lo_ready, 2 * k + 6)
                        load_w(w_cat, (s + 2) % NW)

            turns(sp, body)
            for k in range(B - 3, B):
                sp.wait_ge(out_ready, k + 1)
                sp.dma_start(out[k], out_sb[k % NO][:]).then_inc(out_stored[k % NO], 16)
            for slot in range(NO):
                sp.wait_ge(out_stored[slot], 16 * (B // NO))

        @block.gpsimd
        def _(pool):
            nc.gpsimd.memset(ident[:], 0.0).then_inc(pool_step, 1)
            nc.gpsimd.memset(ident_bf[:], 0.0).then_inc(pool_step, 1)
            nc.gpsimd.memset(penalty[:], 0.0).then_inc(pool_step, 1)
            pool.wait_ge(pool_step, 3)
            nc.gpsimd.affine_select(out=ident[:], in_=ident[:], compare_op=ALU.not_equal, fill=1.0, base=0,
                                    pattern=[[-1, P]], channel_multiplier=1).then_inc(consts_ready, 1)
            nc.gpsimd.affine_select(out=ident_bf[:], in_=ident_bf[:], compare_op=ALU.not_equal, fill=1.0,
                                    base=0, pattern=[[-1, P]], channel_multiplier=1).then_inc(consts_ready, 1)
            nc.gpsimd.affine_select(out=penalty[:, 0, :], in_=penalty[:, 0, :], compare_op=ALU.is_ge,
                                    fill=MASKED, base=0, pattern=[[-1, S]], channel_multiplier=1)\
                .then_inc(consts_ready, 1)
            nc.gpsimd.affine_select(out=penalty[:, 1, :], in_=penalty[:, 1, :], compare_op=ALU.is_ge,
                                    fill=MASKED, base=0, pattern=[[1, S]], channel_multiplier=-1)\
                .then_inc(consts_ready, 1)
            nc.gpsimd.affine_select(out=penalty[:, 2, :], in_=penalty[:, 2, :], compare_op=ALU.not_equal,
                                    fill=MASKED, base=0, pattern=[[-1, S]], channel_multiplier=1)\
                .then_inc(consts_ready, 1)
            nc.gpsimd.iota(row_i[:, 0:1], pattern=[[0, 1]], base=2 - S, channel_multiplier=1)\
                .then_inc(consts_ready, 1)
            nc.gpsimd.iota(row_i[:, 1:2], pattern=[[0, 1]], base=1, channel_multiplier=-1)\
                .then_inc(consts_ready, 1)

        @block.scalar
        def _(act):
            def split_xT_hi(n, slot, q):
                act.wait_ge(xT_done, n + 1)
                nc.scalar.activation(xT_hi[q][:, :, slot * S:(slot + 1) * S],
                                     ps_xT[slot % 2][:].rearrange("p (c s) -> p c s", c=DC), ACT.Copy)\
                    .then_inc(xT_hi_ready, 1)

            def split_w_hi(slot, half):
                h = slice(half * HALF, (half + 1) * HALF)
                nc.scalar.activation(w_hi[slot][:, h, :], w_raw[slot][:, h, :], ACT.Copy)\
                    .then_inc(w_hi_ready, 1)

            def tanh_group(g):
                act.wait_ge(pre_done, g + 1)
                nc.scalar.activation(attn[:], ps_mix[:], ACT.Tanh, bias=b1_col[:]).then_inc(attn_ready, 1)

            def exp_group(g):
                act.wait_ge(neg_max_ready, g + 1)
                for i in range(G):
                    last = nc.scalar.activation(probs[:, i, :], ps_scores[:, i * S:(i + 1) * S], ACT.Exp,
                                                bias=neg_max[:, i:i + 1], accum_out=row_sum[:, i:i + 1])
                last.then_inc(exp_ready, 1)

            def split_z_hi(k, s):
                act.wait_ge(z_ready, k + 1)
                nc.scalar.activation(z_hi[s % NZ][:], z_sb[s % NZ][:], ACT.Copy).then_inc(z_hi_ready, 1)

            def copy_out(k, s):
                act.wait_ge(pz_done, k + 1)
                nc.scalar.activation(out_sb[s % NO][:], ps_pz[s % 2][:], ACT.Copy).then_inc(out_ready, 1)

            for i in range(G):
                if i == 2:
                    act.wait_ge(small_in[1], 16)
                    nc.scalar.activation(w1_hi[:], w1_raw[:], ACT.Copy).then_inc(w1_hi_ready, 1)
                split_xT_hi(i, i, 0)
            act.wait_ge(w_in[0], 16)
            split_w_hi(0, 0)
            split_w_hi(0, 1)
            act.wait_ge(small_in[5], 16)
            nc.scalar.activation(b_hi[:], b_raw[:], ACT.Copy).then_inc(b_hi_ready, 1)
            act.wait_ge(small_in[2], 16)
            tanh_group(0)
            act.wait_ge(w_in[1], 16)
            split_w_hi(1, 0)
            split_w_hi(1, 1)

            def body(t, k0, first, last):
                for s in range(TURN):
                    k, b, q = k0 + s, s % G, s // G
                    nxt = k - b + G
                    g = 2 * t + q
                    has_next = not (last and q == 1)
                    has_w = not (last and s + 2 >= TURN)
                    start = first and s == 0
                    if start:
                        split_xT_hi(nxt, 0, 1 - q)
                        split_xT_hi(nxt + 1, 1, 1 - q)
                    if b == 3 and has_next:
                        tanh_group(g + 1)
                    if has_w:
                        act.wait_ge(w_in[(s + 2) % NW], 16 * ((TURN // NW) * t + (s + 2) // NW + 1))
                        if not first or s >= 2:
                            act.wait_ge(xw_done, k - 1)
                        split_w_hi((s + 2) % NW, 0)
                    if b == 0:
                        exp_group(g)
                    if b == 0 and has_next and not start:
                        if not first or q == 1:
                            act.wait_ge(xw_done, k)
                        split_xT_hi(nxt, 0, 1 - q)
                    if b == 1 and has_next:
                        split_xT_hi(nxt + 2, 2, 1 - q)
                    if b == 2:
                        act.wait_ge(mix_ready, g + 1)
                        if not first:
                            act.wait_ge(pz_done, k - 6)
                        nc.scalar.activation(mix_hi[q][:], mix[:], ACT.Copy).then_inc(mix_hi_ready, 1)
                    if not first or s >= 1:
                        if not first or s >= 1 + NZ:
                            act.wait_ge(pz_done, k - 2)
                        split_z_hi(k - 1, (s - 1) % TURN)
                    if not first or s >= 3:
                        if not first or s >= 3 + NO:
                            act.wait_ge(out_stored[(s - 3) % NO],
                                        16 * ((TURN // NO) * t + (s - 3) // NO))
                        copy_out(k - 3, (s - 3) % TURN)
                    if has_w:
                        split_w_hi((s + 2) % NW, 1)
                    if b == 0 and has_next and not start:
                        split_xT_hi(nxt + 1, 1, 1 - q)
                    if b == 1 and has_next:
                        split_xT_hi(nxt + 3, 3, 1 - q)

            turns(act, body)
            act.wait_ge(pz_done, B - NZ)
            split_z_hi(B - 1, TURN - 1)
            for k in range(B - 3, B):
                act.wait_ge(out_stored[k % NO], 16 * (k // NO))
                copy_out(k, k % TURN)

        @block.vector
        def _(dve):
            def split_xT_lo(n, slot, q):
                dve.wait_ge(xT_hi_ready, n + 1)
                part = slice(slot * S, (slot + 1) * S)
                nc.vector.tensor_tensor(xT_lo[q][:, :, part],
                                        ps_xT[slot % 2][:].rearrange("p (c s) -> p c s", c=DC),
                                        xT_hi[q][:, :, part].bitcast(F32), ALU.subtract)\
                    .then_inc(xT_lo_ready, 1)

            def split_w_lo(n, slot, half):
                dve.wait_ge(w_hi_ready, 2 * n + half + 1)
                h = slice(half * HALF, (half + 1) * HALF)
                nc.vector.tensor_tensor(w_lo[slot][:, h, :], w_raw[slot][:, h, :],
                                        w_hi[slot][:, h, :].bitcast(F32), ALU.subtract)\
                    .then_inc(w_lo_ready, 1)

            def max_group(g):
                dve.wait_ge(scores_done, g + 1)
                nc.vector.tensor_reduce(neg_max[:], ps_scores[:].rearrange("p (b l) -> p b l", b=G),
                                        AXIS_X, ALU.max, negate=True).then_inc(neg_max_ready, 1)

            def scale_group(g):
                dve.wait_ge(exp_ready, g + 1)
                nc.vector.tensor_tensor(row_div[:], row_sum[:], seen[:, bass.ds(G * g, G)], ALU.mult)\
                    .then_inc(div_ready, 1)
                dve.wait_ge(div_ready, g + 1)
                nc.vector.reciprocal(row_scale[:], row_div[:]).then_inc(scale_ready, 1)
                dve.wait_ge(scale_ready, g + 1)
                nc.vector.tensor_tensor(probs[:], probs[:],
                                        row_scale[:].rearrange("p (b a) -> p b a", a=1).to_broadcast([P, G, S]),
                                        ALU.mult).then_inc(probs_ready, 1)

            def make_z(k, s):
                dve.wait_ge(xw_done, k + 1)
                nc.vector.tensor_tensor(z_sb[s % NZ][:], ps_xw[s % 2][:], x_sb[s % NX][:], ALU.add)\
                    .then_inc(z_ready, 1)

            def split_z_lo(k, s):
                dve.wait_ge(z_hi_ready, k + 1)
                nc.vector.tensor_tensor(z_lo[s % NZ][:], z_sb[s % NZ][:], z_hi[s % NZ][:].bitcast(F32),
                                        ALU.subtract).then_inc(z_lo_ready, 1)

            def make_mix(g):
                dve.wait_ge(probsT_done, g + 1)
                nc.vector.tensor_tensor(mix[:], ps_mix[:].rearrange("p (b j) -> p b j", b=G),
                                        ident[:].rearrange("p (a j) -> p a j", a=1).to_broadcast([P, G, S]),
                                        ALU.add).then_inc(mix_ready, 1)

            def split_mix_lo(g, q):
                dve.wait_ge(mix_hi_ready, g + 1)
                nc.vector.tensor_tensor(mix_lo[q][:], mix[:], mix_hi[q][:].bitcast(F32), ALU.subtract)\
                    .then_inc(mix_lo_ready, 1)

            nc.vector.memset(ones[:].bitcast(F32), 1.0).then_inc(pe_consts_ready, 1)
            for i in range(G):
                if i == 2:
                    dve.wait_ge(small_in[3], 16)
                    nc.vector.tensor_copy(v_wide[:], v_col[:].to_broadcast([P, P])).then_inc(pe_consts_ready, 1)
                    dve.wait_ge(w1_hi_ready, 1)
                    nc.vector.tensor_tensor(w1_lo[:], w1_raw[:], w1_hi[:].bitcast(F32), ALU.subtract)\
                        .then_inc(pe_consts_ready, 1)
                split_xT_lo(i, i, 0)
            dve.wait_ge(small_in[4], 16)
            dve.wait_ge(consts_ready, 7)
            nc.vector.tensor_scalar(is_prefix[:], type_all[:], 0.0, None, ALU.is_equal).then_inc(setup_step, 1)
            nc.vector.tensor_scalar(is_postfix[:], type_all[:], 1.0, None, ALU.is_equal).then_inc(setup_step, 1)
            nc.vector.tensor_copy(row_f[:], row_i[:]).then_inc(setup_step, 1)
            dve.wait_ge(setup_step, 3)
            nc.vector.tensor_scalar(type_tmp[:], is_prefix[:], -2.0, 2.0, ALU.mult, ALU.add).then_inc(setup_step, 1)
            dve.wait_ge(setup_step, 4)
            nc.vector.tensor_tensor(type_row[:], type_tmp[0:1, :], is_postfix[0:1, :], ALU.subtract)\
                .then_inc(pe_consts_ready, 1)
            nc.vector.tensor_scalar(is_prefix[:], is_prefix[:], row_f[:, 0:1], float(S - 1), ALU.mult, ALU.add)\
                .then_inc(setup_step, 1)
            dve.wait_ge(setup_step, 5)
            nc.vector.scalar_tensor_tensor(seen[:], is_postfix[:], row_f[:, 1:2], is_prefix[:],
                                           ALU.mult, ALU.add).then_inc(setup_step, 1)
            split_w_lo(0, 0, 0)
            split_w_lo(0, 0, 1)
            dve.wait_ge(b_hi_ready, 1)
            nc.vector.tensor_tensor(b_lo[:], b_raw[:], b_hi[:].bitcast(F32), ALU.subtract)\
                .then_inc(b_parts_ready, 1)
            split_w_lo(1, 1, 0)
            split_w_lo(1, 1, 1)
            max_group(0)
            dve.wait_ge(setup_step, 6)

            def body(t, k0, first, last):
                for s in range(TURN):
                    k, b, q = k0 + s, s % G, s // G
                    nxt = k - b + G
                    g = 2 * t + q
                    has_next = not (last and q == 1)
                    has_w = not (last and s + 2 >= TURN)
                    start = first and s == 0
                    if start:
                        split_xT_lo(nxt, 0, 1 - q)
                        split_xT_lo(nxt + 1, 1, 1 - q)
                    if b == 1 and has_next and not (first and s == 1):
                        split_xT_lo(nxt + 1, 1, 1 - q)
                    if b == 2 and has_next:
                        split_xT_lo(nxt + 3, 3, 1 - q)
                    if not first or s >= 1:
                        make_z(k - 1, (s - 1) % TURN)
                    if has_w:
                        split_w_lo(k + 2, (s + 2) % NW, 0)
                    if b == 0:
                        scale_group(g)
                    if b == 0 and has_next and not start:
                        split_xT_lo(nxt, 0, 1 - q)
                    if b == 1 and has_next:
                        split_xT_lo(nxt + 2, 2, 1 - q)
                    if b == 2:
                        split_mix_lo(g, q)
                    if not first or s >= 1:
                        split_z_lo(k - 1, (s - 1) % TURN)
                    if b == 1:
                        make_mix(g)
                    if has_w:
                        split_w_lo(k + 2, (s + 2) % NW, 1)
                    if b == 3 and has_next:
                        max_group(g + 1)

            turns(dve, body)
            make_z(B - 1, TURN - 1)
            split_z_lo(B - 1, TURN - 1)

        @block.tensor
        def _(pe):
            def transpose_x(n, slot, uses, free):
                pe.wait_ge(x_in[uses[0]], uses[1])
                if free:
                    pe.wait_ge(xT_lo_ready, n - 1)
                for c in range(DC):
                    last = nc.tensor.transpose(ps_xT[slot % 2][:, c * S:(c + 1) * S],
                                               x_sb[uses[0]][:, c * P:(c + 1) * P], ident[:])
                last.then_inc(xT_done, 1)

            def hidden_group(g, q):
                pe.wait_ge(xT_lo_ready, G * g + G)
                passes = [(w1_hi, xT_hi), (w1_hi, xT_lo), (w1_lo, xT_hi)]
                for c in range(DC):
                    for i, (wp, xp) in enumerate(passes):
                        last = nc.tensor.matmul(ps_mix[:], wp[:, c, :], xp[q][:, c, :],
                                                start=(c == 0 and i == 0), stop=(c == DC - 1 and i == 2))
                last.then_inc(pre_done, 1)

            def load_kind(n):
                return pe.value_load(type_row[0:1, bass.ds(n, 1)], min_val=0, max_val=2)

            def scores_group(g, kinds):
                pe.wait_ge(attn_ready, g + 1)
                nc.tensor.matmul(ps_scores[:], v_wide[:], attn[:], start=True, stop=False)
                for i in range(G):
                    last = nc.tensor.matmul(
                        ps_scores[:, i * S:(i + 1) * S], ident_bf[:],
                        penalty[:, bass.ds(kinds[i], 1), :].rearrange("p a l -> p (a l)"),
                        start=False, stop=(i == G - 1))
                last.then_inc(scores_done, 1)

            def xw_half(s, q, slot, half):
                y, ws = ps_xw[s % 2], s % NW
                for c in range(half * HALF, (half + 1) * HALF):
                    xs = slice(slot * S, (slot + 1) * S)
                    nc.tensor.matmul(y[:], xT_hi[q][:, c, xs], w_hi[ws][:, c, :], start=(c == 0), stop=False)
                    nc.tensor.matmul(y[:], xT_hi[q][:, c, xs], w_lo[ws][:, c, :], start=False, stop=False)
                    last = nc.tensor.matmul(y[:], xT_lo[q][:, c, xs], w_hi[ws][:, c, :],
                                            start=False, stop=(c == DC - 1))
                return last

            def pz(k, s, bias_count, first):
                q, b = s // G, s % G
                pe.wait_ge(bias_in[s % NB], bias_count)
                if not first:
                    pe.wait_ge(out_ready, k - 1)
                o, js = ps_pz[s % 2], slice(b, b + 1)
                mh = mix_hi[q][:, js, :].rearrange("p a j -> p (a j)")
                ml = mix_lo[q][:, js, :].rearrange("p a j -> p (a j)")
                nc.tensor.matmul(o[:], ones[:], bias_rows[s % NB][:], start=True, stop=False)
                pe.wait_ge(z_lo_ready, k + 1)
                nc.tensor.matmul(o[:], mh, z_hi[s % NZ][:], start=False, stop=False)
                nc.tensor.matmul(o[:], mh, z_lo[s % NZ][:], start=False, stop=False)
                nc.tensor.matmul(o[:], ml, z_hi[s % NZ][:], start=False, stop=True).then_inc(pz_done, 1)

            pe.wait_ge(consts_ready, 7)
            for i in range(G):
                transpose_x(i, i, (i, 16), i >= 2)
            pe.wait_ge(pe_consts_ready, 3)
            hidden_group(0, 0)
            pe.wait_ge(pe_consts_ready, 4)
            first_kinds = [load_kind(i) for i in range(G)]

            def body(t, k0, first, last):
                for s in range(TURN):
                    k, b, q = k0 + s, s % G, s // G
                    nxt = k - b + G
                    g = 2 * t + q
                    if b == 0:
                        kinds = []
                    has_next = not (last and q == 1)

                    def next_transpose(i):
                        slot_x = (G * (1 - q) + i) % NX
                        transpose_x(nxt + i, i, (slot_x, 16 * (t + q + 1)), True)

                    if b < 2 and has_next and not (first and s == 0):
                        next_transpose(2 * b)
                    if not first or s >= 2:
                        pe.wait_ge(z_ready, k - 1)
                    pe.wait_ge(w_lo_ready, 2 * k + 1)
                    xw_half(s, q, b, 0)
                    if has_next:
                        kinds.append(load_kind(nxt + b))
                    if first and s == 0:
                        scores_group(0, first_kinds)
                        next_transpose(0)
                    if b == 1:
                        pe.wait_ge(probs_ready, g + 1)
                        for i in range(G):
                            end = nc.tensor.transpose(ps_mix[:, i * S:(i + 1) * S], probs[:, i, :], ident[:])
                        end.then_inc(probsT_done, 1)
                    if b < 2 and has_next:
                        next_transpose(2 * b + 1)
                    if b == 3 and has_next:
                        pe.wait_ge(exp_ready, g + 1)
                        scores_group(g + 1, kinds)
                    pe.wait_ge(w_lo_ready, 2 * k + 2)
                    xw_half(s, q, b, 1).then_inc(xw_done, 1)
                    if b == 2 and has_next:
                        pe.wait_ge(mix_ready, g + 1)
                        hidden_group(g + 1, 1 - q)
                    if b == 2:
                        pe.wait_ge(mix_lo_ready, g + 1)
                    if not first or s >= 2:
                        pz(k - 2, (s - 2) % TURN, 16 * (2 * t + (s - 2) // G + 1), first and s <= 3)

            turns(pe, body)
            for k in (B - 2, B - 1):
                pz(k, k % TURN, 16 * GROUPS, False)


_INS = ["x", "itok_B_0_2", "itok_B_0_63", "L0_cond_W1", "L0_cond_b1", "L0_cond_v", "L1_cond_W", "L1_cond_b"]


def kernel(**inputs):
    import numpy as np
    import concourse.bacc as bacc
    from concourse.bass_utils import run_bass_kernel_spmd

    nc = bacc.Bacc("TRN2", target_bir_lowering=False, num_devices=1)
    arrays, args = {}, []
    for name in _INS:
        a = np.ascontiguousarray(inputs[name])
        arrays[f"in_{name}"] = a
        args.append(nc.dram_tensor(f"in_{name}", a.shape, mybir.dt.from_np(a.dtype), kind="ExternalInput").ap())
    out = nc.dram_tensor("out", arrays["in_x"].shape, F32, kind="ExternalOutput").ap()
    program(nc, *args, out)
    r = run_bass_kernel_spmd(nc, [arrays], core_ids=[0])
    return r.results[0]["out"]
```

```python
from contextlib import ExitStack

import concourse.bass as bass
from concourse import mybir

ALU = mybir.AluOpType
ACT = mybir.ActivationFunctionType
AXIS_X = mybir.AxisListType.X
F32 = mybir.dt.float32
F32R = mybir.dt.float32r
BF16 = mybir.dt.bfloat16
I32 = mybir.dt.int32

MASKED = -1e30


def program(nc, x, types, cats, w1, b1, v, w, bias, out):
    B, S, D = x.shape
    A = w1.shape[1]
    C = w.shape[0]
    P = 128
    assert S == P and A == P and D % P == 0
    DC = D // P
    HALF = DC // 2
    G = 4
    TURN = 2 * G
    GROUPS = B // G
    TURNS = B // TURN
    NX, NW, NZ, NO, NB = TURN, 4, 2, 4, 4

    ctx = ExitStack()
    with ctx:
        def sb(name, shape, dt):
            return ctx.enter_context(nc.sbuf_tensor(name, shape, dt))

        def bank(name):
            return ctx.enter_context(nc.psum_tensor(name, [P, 512], F32))

        def sem(name):
            return ctx.enter_context(nc.semaphore(name))

        x_sb = [sb(f"x_sb{i}", [P, D], F32) for i in range(NX)]
        z_sb = [sb(f"z_sb{i}", [P, D], F32) for i in range(NZ)]
        z_hi = [sb(f"z_hi{i}", [P, D], F32R) for i in range(NZ)]
        z_lo = [sb(f"z_lo{i}", [P, D], F32R) for i in range(NZ)]
        out_sb = [sb(f"out_sb{i}", [P, D], F32) for i in range(NO)]
        xT_hi = [sb(f"xT_hi{i}", [P, DC, G * S], F32R) for i in range(2)]
        xT_lo = [sb(f"xT_lo{i}", [P, DC, G * S], F32R) for i in range(2)]
        w_raw = [sb(f"w_raw{i}", [P, DC, D], F32) for i in range(NW)]
        w_hi = [sb(f"w_hi{i}", [P, DC, D], F32R) for i in range(NW)]
        w_lo = [sb(f"w_lo{i}", [P, DC, D], F32R) for i in range(NW)]
        bias_rows = [sb(f"bias_rows{i}", [2, D], F32R) for i in range(NB)]
        attn = sb("attn", [P, G * S], F32)
        attn_hi = sb("attn_hi", [P, G * S], F32R)
        attn_lo = sb("attn_lo", [P, G * S], F32R)
        probs = sb("probs", [P, G, S], F32)
        mix = sb("mix", [P, G, S], F32)
        mix_hi = [sb(f"mix_hi{i}", [P, G, S], F32R) for i in range(2)]
        mix_lo = [sb(f"mix_lo{i}", [P, G, S], F32R) for i in range(2)]
        neg_max = sb("neg_max", [P, G], F32)
        row_sum = sb("row_sum", [P, G], F32)
        row_div = sb("row_div", [P, G], F32)
        row_scale = sb("row_scale", [P, G], F32)

        w1_raw = sb("w1_raw", [P, DC, A], F32)
        w1_hi = sb("w1_hi", [P, DC, A], F32R)
        w1_lo = sb("w1_lo", [P, DC, A], F32R)
        b1_col = sb("b1_col", [P, 1], F32)
        v_col = sb("v_col", [P, 1], F32)
        v_hi = sb("v_hi", [P, P], F32R)
        v_lo = sb("v_lo", [P, P], F32R)
        ident = sb("ident", [P, P], F32)
        ident_bf = sb("ident_bf", [P, P], BF16)
        penalty = sb("penalty", [P, 3, S], BF16)
        ones = sb("ones", [2, P], F32R)
        warm = sb("warm", [P, 256], BF16)
        b_raw = sb("b_raw", [C, D], F32)
        b_hi = sb("b_hi", [C, D], F32R)
        b_lo = sb("b_lo", [C, D], F32R)
        cat_row = sb("cat_row", [1, B], I32)
        type_all = sb("type_all", [P, B], I32)
        is_prefix = sb("is_prefix", [P, B], F32)
        is_postfix = sb("is_postfix", [P, B], F32)
        type_tmp = sb("type_tmp", [P, B], F32)
        type_row = sb("type_row", [1, B], I32)
        row_i = sb("row_i", [P, 2], I32)
        row_f = sb("row_f", [P, 2], F32)
        seen = sb("seen", [P, B], F32)
        b_split = nc.dram_tensor("b_split", (C, 2, D), F32, kind="Internal").ap()

        ps_xT = [bank("ps_xT0"), bank("ps_xT1")]
        ps_mix = bank("ps_mix")
        ps_scores = bank("ps_scores")
        ps_xw = [bank("ps_xw0"), bank("ps_xw1")]
        ps_pz = [bank("ps_pz0"), bank("ps_pz1")]

        small_in = [sem(f"small_in{i}") for i in range(6)]
        x_in = [sem(f"x_in{i}") for i in range(NX)]
        w_in = [sem(f"w_in{i}") for i in range(NW)]
        bias_in = [sem(f"bias_in{i}") for i in range(NB)]
        out_stored = [sem(f"out_stored{i}") for i in range(NO)]
        b_split_stored = sem("b_split_stored")
        pool_step = sem("pool_step")
        consts_ready = sem("consts_ready")
        warm_ready = sem("warm_ready")
        setup_step = sem("setup_step")
        b_hi_ready = sem("b_hi_ready")
        v_hi_ready = sem("v_hi_ready")
        b_parts_ready = sem("b_parts_ready")
        w1_hi_ready = sem("w1_hi_ready")
        pe_consts_ready = sem("pe_consts_ready")
        xT_done = sem("xT_done")
        xT_hi_ready = sem("xT_hi_ready")
        xT_lo_ready = sem("xT_lo_ready")
        w_hi_ready = sem("w_hi_ready")
        w_lo_ready = sem("w_lo_ready")
        pre_done = sem("pre_done")
        attn_ready = sem("attn_ready")
        attn_hi_ready = sem("attn_hi_ready")
        attn_lo_ready = sem("attn_lo_ready")
        scores_done = sem("scores_done")
        neg_max_ready = sem("neg_max_ready")
        exp_ready = sem("exp_ready")
        div_ready = sem("div_ready")
        scale_ready = sem("scale_ready")
        probs_ready = sem("probs_ready")
        probsT_done = sem("probsT_done")
        mix_ready = sem("mix_ready")
        mix_hi_ready = sem("mix_hi_ready")
        mix_lo_ready = sem("mix_lo_ready")
        xw_done = sem("xw_done")
        z_ready = sem("z_ready")
        z_hi_ready = sem("z_hi_ready")
        z_lo_ready = sem("z_lo_ready")
        pz_done = sem("pz_done")
        out_ready = sem("out_ready")

        block = ctx.enter_context(nc.Block())

        def turns(eng, body):
            body(0, 0, True, False)
            with eng.Fori(1, TURNS - 1) as t:
                body(t, TURN * t, False, False)
            body(TURNS - 1, TURN * (TURNS - 1), False, True)

        @block.sync
        def _(sp):
            def load_x(n, slot):
                sp.dma_start(x_sb[slot][:], x[bass.ds(n, 1)].rearrange("a s d -> (a s) d"))\
                    .then_inc(x_in[slot], 16)

            def load_w(cat, slot):
                sp.dma_start(w_raw[slot][:], w[bass.ds(cat, 1)].rearrange("a (c p) h -> p (a c) h", p=P))\
                    .then_inc(w_in[slot], 16)

            def load_bias(cat, slot):
                sp.dma_start(bias_rows[slot][:].bitcast(F32), b_split[bass.ds(cat, 1)].rearrange("a t h -> (a t) h"))\
                    .then_inc(bias_in[slot], 16)

            sp.dma_start(cat_row[:], cats.rearrange("(a n) -> a n", a=1)).then_inc(small_in[0], 16)
            load_x(0, 0)
            sp.dma_start(w1_raw[:], w1.rearrange("(c p) a -> p c a", p=P)).then_inc(small_in[1], 16)
            load_x(1, 1)
            sp.wait_ge(small_in[0], 16)
            first_cats = [sp.value_load(cat_row[0:1, 0:1], min_val=0, max_val=C - 1)]
            load_w(first_cats[0], 0)
            sp.dma_start(v_col[:], v.rearrange("(p a) -> p a", a=1)).then_inc(small_in[3], 16)
            load_x(2, 2)
            load_x(3, 3)
            first_cats += [sp.value_load(cat_row[0:1, 1:2], min_val=0, max_val=C - 1)]
            load_w(first_cats[1], 1)
            load_x(4, 4)
            load_x(5, 5)
            first_cats += [sp.value_load(cat_row[0:1, k:k + 1], min_val=0, max_val=C - 1)
                           for k in range(2, NW + 1)]
            load_w(first_cats[2], 2)
            load_x(6, 6)
            load_x(7, 7)
            load_w(first_cats[3], 3)
            sp.wait_ge(b_parts_ready, 1)
            sp.dma_start(b_split[:, 0, :], b_hi[:].bitcast(F32)).then_inc(b_split_stored, 16)
            sp.dma_start(b_split[:, 1, :], b_lo[:].bitcast(F32)).then_inc(b_split_stored, 16)
            sp.wait_ge(w_lo_ready, 2)
            load_w(first_cats[NW], 0)
            sp.wait_ge(b_split_stored, 32)
            load_bias(first_cats[0], 0)

            def body(t, k0, first, last):
                for s in range(TURN):
                    k = k0 + s
                    has_w = not (last and s + NW + 1 >= TURN)
                    has_bias = not (last and s + 1 >= TURN)
                    if has_w:
                        w_cat = sp.value_load(cat_row[0:1, bass.ds(k + NW + 1, 1)], min_val=0, max_val=C - 1)
                    if has_bias:
                        bias_cat = sp.value_load(cat_row[0:1, bass.ds(k + 1, 1)], min_val=0, max_val=C - 1)
                    if not (first and s == 0) and not (last and s + NX - 1 >= TURN):
                        sp.wait_ge(z_ready, k)
                        load_x(k + NX - 1, (s - 1) % NX)
                    if not first or s >= 3:
                        sp.wait_ge(out_ready, k - 2)
                        sp.dma_start(out[bass.ds(k - 3, 1)].rearrange("a s d -> (a s) d"),
                                     out_sb[(s - 3) % NO][:]).then_inc(out_stored[(s - 3) % NO], 16)
                    if has_bias:
                        load_bias(bias_cat, (s + 1) % NB)
                    if has_w:
                        sp.wait_ge(w_lo_ready, 2 * k + 4)
                        load_w(w_cat, (s + 1) % NW)

            turns(sp, body)
            for k in range(B - 3, B):
                sp.wait_ge(out_ready, k + 1)
                sp.dma_start(out[k], out_sb[k % NO][:]).then_inc(out_stored[k % NO], 16)
            for slot in range(NO):
                sp.wait_ge(out_stored[slot], 16 * (B // NO))

        @block.gpsimd
        def _(pool):
            pool.dma_start(type_all[:], types.rearrange("(a n) -> a n", a=1).to_broadcast([P, B]))\
                .then_inc(small_in[4], 16)
            nc.gpsimd.memset(ident[:], 0.0).then_inc(pool_step, 1)
            nc.gpsimd.memset(ident_bf[:], 0.0).then_inc(pool_step, 1)
            nc.gpsimd.memset(penalty[:], 0.0).then_inc(pool_step, 1)
            pool.wait_ge(pool_step, 3)
            nc.gpsimd.affine_select(out=ident[:], in_=ident[:], compare_op=ALU.not_equal, fill=1.0, base=0,
                                    pattern=[[-1, P]], channel_multiplier=1).then_inc(consts_ready, 1)
            nc.gpsimd.affine_select(out=ident_bf[:], in_=ident_bf[:], compare_op=ALU.not_equal, fill=1.0,
                                    base=0, pattern=[[-1, P]], channel_multiplier=1).then_inc(consts_ready, 1)
            nc.gpsimd.affine_select(out=penalty[:, 0, :], in_=penalty[:, 0, :], compare_op=ALU.is_ge,
                                    fill=MASKED, base=0, pattern=[[-1, S]], channel_multiplier=1)\
                .then_inc(consts_ready, 1)
            nc.gpsimd.affine_select(out=penalty[:, 1, :], in_=penalty[:, 1, :], compare_op=ALU.is_ge,
                                    fill=MASKED, base=0, pattern=[[1, S]], channel_multiplier=-1)\
                .then_inc(consts_ready, 1)
            nc.gpsimd.affine_select(out=penalty[:, 2, :], in_=penalty[:, 2, :], compare_op=ALU.not_equal,
                                    fill=MASKED, base=0, pattern=[[-1, S]], channel_multiplier=1)\
                .then_inc(consts_ready, 1)
            nc.gpsimd.iota(row_i[:, 0:1], pattern=[[0, 1]], base=2 - S, channel_multiplier=1)\
                .then_inc(consts_ready, 1)
            nc.gpsimd.iota(row_i[:, 1:2], pattern=[[0, 1]], base=1, channel_multiplier=-1)\
                .then_inc(consts_ready, 1)
            pool.dma_start(b_raw[:], bias).then_inc(small_in[5], 16)
            pool.dma_start(b1_col[:], b1.rearrange("(p a) -> p a", a=1)).then_inc(small_in[2], 16)

        @block.scalar
        def _(act):
            def split_xT_hi(n, slot, q):
                act.wait_ge(xT_done, n + 1)
                nc.scalar.activation(xT_hi[q][:, :, slot * S:(slot + 1) * S],
                                     ps_xT[slot % 2][:].rearrange("p (c s) -> p c s", c=DC), ACT.Copy)\
                    .then_inc(xT_hi_ready, 1)

            def split_w_hi(slot, half):
                h = slice(half * HALF, (half + 1) * HALF)
                nc.scalar.activation(w_hi[slot][:, h, :], w_raw[slot][:, h, :], ACT.Copy)\
                    .then_inc(w_hi_ready, 1)

            def tanh_group(g):
                act.wait_ge(pre_done, g + 1)
                nc.scalar.activation(attn[:], ps_mix[:], ACT.Tanh, bias=b1_col[:]).then_inc(attn_ready, 1)
                act.wait_ge(attn_ready, g + 1)
                nc.scalar.activation(attn_hi[:], attn[:], ACT.Copy).then_inc(attn_hi_ready, 1)

            def exp_group(g):
                act.wait_ge(neg_max_ready, g + 1)
                for i in range(G):
                    last = nc.scalar.activation(probs[:, i, :], ps_scores[:, i * S:(i + 1) * S], ACT.Exp,
                                                bias=neg_max[:, i:i + 1], accum_out=row_sum[:, i:i + 1])
                last.then_inc(exp_ready, 1)

            def scale_group(g):
                act.wait_ge(scale_ready, g + 1)
                for i in range(G):
                    last = nc.scalar.activation(probs[:, i, :], probs[:, i, :], ACT.Copy, scale=row_scale[:, i:i + 1])
                last.then_inc(probs_ready, 1)

            def split_mix_hi(g, q, used):
                act.wait_ge(mix_ready, g + 1)
                if used is not None:
                    act.wait_ge(pz_done, used)
                nc.scalar.activation(mix_hi[q][:], mix[:], ACT.Copy).then_inc(mix_hi_ready, 1)

            def split_z_hi(k, s):
                act.wait_ge(z_ready, k + 1)
                nc.scalar.activation(z_hi[s % NZ][:], z_sb[s % NZ][:], ACT.Copy).then_inc(z_hi_ready, 1)

            def copy_out(k, s, bank):
                act.wait_ge(pz_done, k + 1)
                nc.scalar.activation(out_sb[s % NO][:], bank[:], ACT.Copy).then_inc(out_ready, 1)

            split_xT_hi(0, 0, 0)
            act.wait_ge(small_in[1], 16)
            nc.scalar.activation(w1_hi[:], w1_raw[:], ACT.Copy).then_inc(w1_hi_ready, 1)
            split_xT_hi(1, 1, 0)
            act.wait_ge(w_in[0], 16)
            split_w_hi(0, 0)
            split_w_hi(0, 1)
            act.wait_ge(small_in[5], 16)
            nc.scalar.activation(b_hi[:], b_raw[:], ACT.Copy).then_inc(b_hi_ready, 1)
            split_xT_hi(2, 2, 0)
            split_xT_hi(3, 3, 0)
            act.wait_ge(w_in[1], 16)
            split_w_hi(1, 0)
            split_w_hi(1, 1)
            act.wait_ge(small_in[2], 16)
            split_xT_hi(4, 0, 1)
            split_xT_hi(5, 1, 1)
            tanh_group(0)

            def body(t, k0, first, last):
                for s in range(TURN):
                    k, b, q = k0 + s, s % G, s // G
                    nxt = k - b + G
                    g = 2 * t + q
                    has_next = not (last and q == 1)
                    has_w = not (last and s + 2 >= TURN)
                    start = first and s == 0
                    early = (first and q == 0) or (last and q == 1)
                    if b == 3 and has_next:
                        tanh_group(g + 1)
                    if b == 2 and early:
                        split_mix_hi(g, q, None if first else k - 6)
                    if has_w and not (first and s == 1):
                        act.wait_ge(w_in[(s + 2) % NW], 16 * ((TURN // NW) * t + (s + 2) // NW + 1))
                        if not first or s >= 2:
                            act.wait_ge(xw_done, k - 1)
                        split_w_hi((s + 2) % NW, 0)
                    whole = b == 0 or (first and 2 <= s <= 3)
                    if has_w and whole:
                        split_w_hi((s + 2) % NW, 1)
                    if start:
                        split_z_hi(0, 0)
                    if b == 0 and not (first and s == G):
                        exp_group(g)
                    if b == 0 and has_next and not start:
                        act.wait_ge(xw_done, k)
                        split_xT_hi(nxt, 0, 1 - q)
                    if first and s == G:
                        exp_group(g)
                    if b == 0 and has_next and not start:
                        split_xT_hi(nxt + 1, 1, 1 - q)
                    if start:
                        act.wait_ge(w_in[3], 16)
                        split_w_hi(3, 0)
                    if b == 0:
                        scale_group(g)
                    if b == 1 and has_next:
                        split_xT_hi(nxt + 2, 2, 1 - q)
                    if b == 2 and not early:
                        split_mix_hi(g, q, None if first else k - 6)
                    if not first or s >= 2:
                        if not first or s >= 1 + NZ:
                            act.wait_ge(pz_done, k - 2)
                        split_z_hi(k - 1, (s - 1) % TURN)
                    if not first or s >= 3:
                        if not first or s >= 3 + NO:
                            act.wait_ge(out_stored[(s - 3) % NO],
                                        16 * ((TURN // NO) * t + (s - 3) // NO))
                        copy_out(k - 3, (s - 3) % TURN, ps_pz[(s - 3) % 2])
                    if has_w and not whole:
                        split_w_hi((s + 2) % NW, 1)
                    if b == 1 and has_next:
                        split_xT_hi(nxt + 3, 3, 1 - q)

            turns(act, body)
            act.wait_ge(pz_done, B - NZ)
            split_z_hi(B - 1, TURN - 1)
            for k in range(B - 3, B):
                act.wait_ge(out_stored[k % NO], 16 * (k // NO))
                copy_out(k, k % TURN, ps_pz[k % 2] if k < B - 2 else ps_xT[k % 2])

        @block.vector
        def _(dve):
            def split_xT_lo(n, slot, q):
                dve.wait_ge(xT_hi_ready, n + 1)
                part = slice(slot * S, (slot + 1) * S)
                nc.vector.tensor_tensor(xT_lo[q][:, :, part],
                                        ps_xT[slot % 2][:].rearrange("p (c s) -> p c s", c=DC),
                                        xT_hi[q][:, :, part].bitcast(F32), ALU.subtract)\
                    .then_inc(xT_lo_ready, 1)

            def split_w_lo(n, slot, half):
                dve.wait_ge(w_hi_ready, 2 * n + half + 1)
                h = slice(half * HALF, (half + 1) * HALF)
                nc.vector.tensor_tensor(w_lo[slot][:, h, :], w_raw[slot][:, h, :],
                                        w_hi[slot][:, h, :].bitcast(F32), ALU.subtract)\
                    .then_inc(w_lo_ready, 1)

            def split_attn_lo(g):
                dve.wait_ge(attn_hi_ready, g + 1)
                nc.vector.tensor_tensor(attn_lo[:], attn[:], attn_hi[:].bitcast(F32), ALU.subtract)\
                    .then_inc(attn_lo_ready, 1)

            def max_group(g):
                dve.wait_ge(scores_done, g + 1)
                nc.vector.tensor_reduce(neg_max[:], ps_scores[:].rearrange("p (b l) -> p b l", b=G),
                                        AXIS_X, ALU.max, negate=True).then_inc(neg_max_ready, 1)

            def row_scale_group(g):
                dve.wait_ge(exp_ready, g + 1)
                nc.vector.tensor_tensor(row_div[:], row_sum[:], seen[:, bass.ds(G * g, G)], ALU.mult)\
                    .then_inc(div_ready, 1)
                dve.wait_ge(div_ready, g + 1)
                nc.vector.reciprocal(row_scale[:], row_div[:]).then_inc(scale_ready, 1)

            def make_z(k, s):
                dve.wait_ge(xw_done, k + 1)
                nc.vector.tensor_tensor(z_sb[s % NZ][:], ps_xw[s % 2][:], x_sb[s % NX][:], ALU.add)\
                    .then_inc(z_ready, 1)

            def split_z_lo(k, s):
                dve.wait_ge(z_hi_ready, k + 1)
                nc.vector.tensor_tensor(z_lo[s % NZ][:], z_sb[s % NZ][:], z_hi[s % NZ][:].bitcast(F32),
                                        ALU.subtract).then_inc(z_lo_ready, 1)

            def make_mix(g):
                dve.wait_ge(probsT_done, g + 1)
                nc.vector.tensor_tensor(mix[:], ps_mix[:].rearrange("p (b j) -> p b j", b=G),
                                        ident[:].rearrange("p (a j) -> p a j", a=1).to_broadcast([P, G, S]),
                                        ALU.add).then_inc(mix_ready, 1)

            def split_mix_lo(g, q):
                dve.wait_ge(mix_hi_ready, g + 1)
                nc.vector.tensor_tensor(mix_lo[q][:], mix[:], mix_hi[q][:].bitcast(F32), ALU.subtract)\
                    .then_inc(mix_lo_ready, 1)

            nc.vector.memset(warm[:], 0.0).then_inc(warm_ready, 1)
            nc.vector.memset(ones[:].bitcast(F32), 1.0).then_inc(pe_consts_ready, 1)
            dve.wait_ge(small_in[4], 16)
            dve.wait_ge(consts_ready, 7)
            nc.vector.tensor_scalar(is_prefix[:], type_all[:], 0.0, None, ALU.is_equal).then_inc(setup_step, 1)
            nc.vector.tensor_scalar(is_postfix[:], type_all[:], 1.0, None, ALU.is_equal).then_inc(setup_step, 1)
            nc.vector.tensor_copy(row_f[:], row_i[:]).then_inc(setup_step, 1)
            dve.wait_ge(setup_step, 3)
            nc.vector.tensor_scalar(type_tmp[:], is_prefix[:], -2.0, 2.0, ALU.mult, ALU.add).then_inc(setup_step, 1)
            dve.wait_ge(setup_step, 4)
            nc.vector.tensor_tensor(type_row[:], type_tmp[0:1, :], is_postfix[0:1, :], ALU.subtract)\
                .then_inc(pe_consts_ready, 1)
            nc.vector.tensor_scalar(is_prefix[:], is_prefix[:], row_f[:, 0:1], float(S - 1), ALU.mult, ALU.add)\
                .then_inc(setup_step, 1)
            dve.wait_ge(setup_step, 5)
            nc.vector.scalar_tensor_tensor(seen[:], is_postfix[:], row_f[:, 1:2], is_prefix[:],
                                           ALU.mult, ALU.add).then_inc(setup_step, 1)
            split_xT_lo(0, 0, 0)
            dve.wait_ge(w1_hi_ready, 1)
            nc.vector.tensor_tensor(w1_lo[:], w1_raw[:], w1_hi[:].bitcast(F32), ALU.subtract)\
                .then_inc(pe_consts_ready, 1)
            split_xT_lo(1, 1, 0)
            split_w_lo(0, 0, 0)
            split_w_lo(0, 0, 1)
            dve.wait_ge(small_in[3], 16)
            nc.vector.tensor_copy(v_hi[:], v_col[:].to_broadcast([P, P])).then_inc(v_hi_ready, 1)
            dve.wait_ge(v_hi_ready, 1)
            nc.vector.tensor_tensor(v_lo[:], v_col[:].to_broadcast([P, P]), v_hi[:].bitcast(F32), ALU.subtract)\
                .then_inc(pe_consts_ready, 1)
            split_xT_lo(2, 2, 0)
            split_xT_lo(3, 3, 0)
            dve.wait_ge(b_hi_ready, 1)
            nc.vector.tensor_tensor(b_lo[:], b_raw[:], b_hi[:].bitcast(F32), ALU.subtract)\
                .then_inc(b_parts_ready, 1)
            split_w_lo(1, 1, 0)
            split_w_lo(1, 1, 1)
            split_xT_lo(4, 0, 1)
            split_xT_lo(5, 1, 1)
            split_attn_lo(0)
            make_z(0, 0)
            max_group(0)
            dve.wait_ge(setup_step, 6)

            def body(t, k0, first, last):
                for s in range(TURN):
                    k, b, q = k0 + s, s % G, s // G
                    nxt = k - b + G
                    g = 2 * t + q
                    has_next = not (last and q == 1)
                    has_w = not (last and s + 2 >= TURN)
                    start = first and s == 0
                    early = (first and q == 0) or (last and q == 1)
                    if b == 2 and has_next and not (first and s == 2):
                        split_xT_lo(nxt + 3, 3, 1 - q)
                    if b == 2 and early:
                        split_mix_lo(g, q)
                    if first and s == 3:
                        split_attn_lo(g + 1)
                    if not first or s >= 2:
                        make_z(k - 1, (s - 1) % TURN)
                    if b == 3 and has_next and not (first and s == 3):
                        split_attn_lo(g + 1)
                    if first and s == 1:
                        split_w_lo(3, 3, 0)
                    if b == 1 and early:
                        make_mix(g)
                    if first and s == G:
                        split_xT_lo(nxt, 0, 1 - q)
                    if has_w and not (first and s == 1):
                        split_w_lo(k + 2, (s + 2) % NW, 0)
                    if start:
                        split_z_lo(0, 0)
                    if b == 0:
                        row_scale_group(g)
                    if b == 0 and has_next and not (first and s <= G):
                        split_xT_lo(nxt, 0, 1 - q)
                    if has_w and b == 0:
                        split_w_lo(k + 2, (s + 2) % NW, 1)
                    if b == 0 and has_next and not start:
                        split_xT_lo(nxt + 1, 1, 1 - q)
                    if b == 1 and has_next:
                        split_xT_lo(nxt + 2, 2, 1 - q)
                    if b == 2 and not early:
                        split_mix_lo(g, q)
                    if not first or s >= 2:
                        split_z_lo(k - 1, (s - 1) % TURN)
                    if first and s == 1:
                        split_xT_lo(nxt + 3, 3, 1 - q)
                    if b == 1 and not early:
                        make_mix(g)
                    if has_w and b != 0:
                        split_w_lo(k + 2, (s + 2) % NW, 1)
                    if b == 3 and has_next:
                        max_group(g + 1)

            turns(dve, body)
            make_z(B - 1, TURN - 1)
            split_z_lo(B - 1, TURN - 1)

        @block.tensor
        def _(pe):
            def transpose_x(n, slot, uses, free):
                pe.wait_ge(x_in[uses[0]], uses[1])
                if free:
                    pe.wait_ge(xT_lo_ready, n - 1)
                for c in range(DC):
                    last = nc.tensor.transpose(ps_xT[slot % 2][:, c * S:(c + 1) * S],
                                               x_sb[uses[0]][:, c * P:(c + 1) * P], ident[:])
                last.then_inc(xT_done, 1)

            def hidden(q, cols):
                passes = [(w1_hi, xT_hi), (w1_hi, xT_lo), (w1_lo, xT_hi)]
                for c in range(DC):
                    for i, (wp, xp) in enumerate(passes):
                        last = nc.tensor.matmul(ps_mix[:, cols], wp[:, c, :], xp[q][:, c, cols],
                                                start=(c == 0 and i == 0), stop=(c == DC - 1 and i == 2))
                return last

            def load_kind(n):
                return pe.value_load(type_row[0:1, bass.ds(n, 1)], min_val=0, max_val=2)

            def scores_group(g, kinds):
                pe.wait_ge(attn_hi_ready, g + 1)
                nc.tensor.matmul(ps_scores[:], v_hi[:], attn_hi[:], start=True, stop=False)
                nc.tensor.matmul(ps_scores[:], v_lo[:], attn_hi[:], start=False, stop=False)
                pe.wait_ge(attn_lo_ready, g + 1)
                nc.tensor.matmul(ps_scores[:], v_hi[:], attn_lo[:], start=False, stop=False)
                for i in range(G):
                    last = nc.tensor.matmul(
                        ps_scores[:, i * S:(i + 1) * S], ident_bf[:],
                        penalty[:, bass.ds(kinds[i], 1), :].rearrange("p a l -> p (a l)"),
                        start=False, stop=(i == G - 1))
                last.then_inc(scores_done, 1)

            def transpose_probs(g):
                pe.wait_ge(probs_ready, g + 1)
                for i in range(G):
                    last = nc.tensor.transpose(ps_mix[:, i * S:(i + 1) * S], probs[:, i, :], ident[:])
                last.then_inc(probsT_done, 1)

            def xw_half(s, q, slot, half):
                y, ws = ps_xw[s % 2], s % NW
                for c in range(half * HALF, (half + 1) * HALF):
                    xs = slice(slot * S, (slot + 1) * S)
                    nc.tensor.matmul(y[:], xT_hi[q][:, c, xs], w_hi[ws][:, c, :], start=(c == 0), stop=False)
                    nc.tensor.matmul(y[:], xT_hi[q][:, c, xs], w_lo[ws][:, c, :], start=False, stop=False)
                    last = nc.tensor.matmul(y[:], xT_lo[q][:, c, xs], w_hi[ws][:, c, :],
                                            start=False, stop=(c == DC - 1))
                return last

            def pz(k, s, bias_count, bank, free):
                q, b = s // G, s % G
                pe.wait_ge(bias_in[s % NB], bias_count)
                if free:
                    pe.wait_ge(out_ready, k - 1)
                o, js = bank, slice(b, b + 1)
                mh = mix_hi[q][:, js, :].rearrange("p a j -> p (a j)")
                ml = mix_lo[q][:, js, :].rearrange("p a j -> p (a j)")
                nc.tensor.matmul(o[:], ones[:], bias_rows[s % NB][:], start=True, stop=False)
                pe.wait_ge(z_hi_ready, k + 1)
                nc.tensor.matmul(o[:], mh, z_hi[s % NZ][:], start=False, stop=False)
                nc.tensor.matmul(o[:], ml, z_hi[s % NZ][:], start=False, stop=False)
                pe.wait_ge(z_lo_ready, k + 1)
                nc.tensor.matmul(o[:], mh, z_lo[s % NZ][:], start=False, stop=True).then_inc(pz_done, 1)

            def warm_up(products):
                for _ in range(products):
                    nc.tensor.matmul(ps_pz[1][:, 0:256], warm[:, 0:P], warm[:], start=True, stop=True)

            pe.wait_ge(warm_ready, 1)
            warm_up(14)
            pe.wait_ge(consts_ready, 1)
            pair = [slice(0, 2 * S), slice(2 * S, 4 * S)]
            transpose_x(0, 0, (0, 16), False)
            transpose_x(1, 1, (1, 16), False)
            pe.wait_ge(pe_consts_ready, 2)
            first_kinds = [load_kind(i) for i in (0, 1)]
            warm_up(4)
            pe.wait_ge(xT_lo_ready, 2)
            hidden(0, pair[0])
            transpose_x(2, 2, (2, 16), True)
            transpose_x(3, 3, (3, 16), True)
            first_kinds += [load_kind(i) for i in (2, 3)]
            warm_up(4)
            pe.wait_ge(w_lo_ready, 1)
            xw_half(0, 0, 0, 0)
            pe.wait_ge(w_lo_ready, 2)
            xw_half(0, 0, 0, 1).then_inc(xw_done, 1)
            transpose_x(4, 0, (4, 16), True)
            transpose_x(5, 1, (5, 16), True)
            pe.wait_ge(xT_lo_ready, 4)
            hidden(0, pair[1]).then_inc(pre_done, 1)

            def body(t, k0, first, last):
                for s in range(TURN):
                    k, b, q = k0 + s, s % G, s // G
                    nxt = k - b + G
                    g = 2 * t + q
                    if b == 0:
                        kinds = []
                    has_next = not (last and q == 1)

                    def next_transpose(i):
                        slot_x = (G * (1 - q) + i) % NX
                        transpose_x(nxt + i, i, (slot_x, 16 * (t + q + 1)), True)

                    if b < 2 and has_next and not (first and s == 0):
                        next_transpose(2 * b)
                    if not first or s >= 2:
                        pe.wait_ge(z_ready, k - 1)
                    start = first and s == 0
                    if not (first and s <= 2):
                        pe.wait_ge(w_lo_ready, 2 * k + 1)
                        xw_half(s, q, b, 0)
                    if has_next:
                        kinds.append(load_kind(nxt + b))
                    if start:
                        pe.wait_ge(w_lo_ready, 3)
                        xw_half(1, 0, 1, 0)
                        pe.wait_ge(pe_consts_ready, 4)
                        pe.wait_ge(consts_ready, 7)
                        scores_group(0, first_kinds)
                    if b == 1 and not (first and s == 1):
                        transpose_probs(g)
                    if b < 2 and has_next and not start:
                        next_transpose(2 * b + 1)
                    if b == 3 and has_next:
                        pe.wait_ge(exp_ready, g + 1)
                        scores_group(g + 1, kinds)
                    if not start:
                        pe.wait_ge(w_lo_ready, 2 * k + 2)
                        xw_half(s, q, b, 1).then_inc(xw_done, 1)
                    if first and s == 1:
                        pe.wait_ge(z_ready, 1)
                        pe.wait_ge(w_lo_ready, 5)
                        xw_half(2, 0, 2, 0)
                        transpose_probs(g)
                    if b == 2 and has_next:
                        pe.wait_ge(mix_ready, g + 1)
                        pe.wait_ge(xT_lo_ready, nxt + G)
                        hidden(1 - q, slice(0, G * S)).then_inc(pre_done, 1)
                    if b == 2:
                        pe.wait_ge(mix_lo_ready, g + 1)
                    if not first or s >= 2:
                        pz(k - 2, (s - 2) % TURN, 16 * (2 * t + (s - 2) // G + 1),
                           ps_pz[s % 2], not (first and s <= 3))

            turns(pe, body)
            for k in (B - 2, B - 1):
                pz(k, k % TURN, 16 * GROUPS, ps_xT[k % 2], False)


_INS = ["x", "itok_B_0_2", "itok_B_0_63", "L0_cond_W1", "L0_cond_b1", "L0_cond_v", "L1_cond_W", "L1_cond_b"]


def kernel(**inputs):
    import numpy as np
    import concourse.bacc as bacc
    from concourse.bass_utils import run_bass_kernel_spmd

    nc = bacc.Bacc("TRN2", target_bir_lowering=False, num_devices=1)
    arrays, args = {}, []
    for name in _INS:
        a = np.ascontiguousarray(inputs[name])
        arrays[f"in_{name}"] = a
        args.append(nc.dram_tensor(f"in_{name}", a.shape, mybir.dt.from_np(a.dtype), kind="ExternalInput").ap())
    out = nc.dram_tensor("out", arrays["in_x"].shape, F32, kind="ExternalOutput").ap()
    program(nc, *args, out)
    r = run_bass_kernel_spmd(nc, [arrays], core_ids=[0])
    return r.results[0]["out"]
```
